# Optimizing a Trainium2 kernel written in Bass

```python
import numpy as np
import jax
import jax.numpy as jnp

def _softmax(x, axis=-1):
    return jax.nn.softmax(x, axis=axis)

def _gelu(x):
    return jax.nn.gelu(x, approximate=True)

def _silu(x):
    return jax.nn.silu(x)

def _sigmoid(x):
    return jax.nn.sigmoid(x)

def _layernorm(x, axis=-1, eps=1e-05):
    m = jnp.mean(x, axis=axis, keepdims=True)
    v = jnp.var(x, axis=axis, keepdims=True)
    return (x - m) / jnp.sqrt(v + eps)

def _scatter_add(tgt, idx, src, axis=0):
    return tgt.at[idx].add(src)

def _segment_sum(src, seg, n):
    return jax.ops.segment_sum(src, seg, n)
kernel_name = 'mk_adj_resnorm_d1_adj_r2_044b35'

def setup_inputs(seed: int=0):
    np.random.seed(seed)
    _w = jnp.asarray

    def _rec_inputs():
        import jax
        import jax.numpy as jnp
        _gk = jax.random.key(seed)
        x = -0.0005207 + 1.001 * jax.random.normal(jax.random.fold_in(_gk, 1), (4096, 128), jnp.float32)
        _a = jax.random.bernoulli(jax.random.fold_in(_gk, 2), 0.00390625, (4096, 4096))
        adj = _a.astype(jnp.int32)
        return (x, adj)
    x, adj = _rec_inputs()

    def _L0_gnn_setup():
        import jax, jax.numpy as jnp
        import numpy as np
        N = 4096
        IN_F = 128
        OUT_F = 128
        ALPHA = 0.2
        NEG_INF = -1000000000000.0

        def _xavier(key, shape, gain=1.414):
            fan_in, fan_out = (shape[0], shape[1])
            bound = gain * np.sqrt(6.0 / (fan_in + fan_out))
            return jax.random.uniform(key, shape, jnp.float32, -bound, bound)
        key = jax.random.key(seed)
        k1, k2, k3, k4 = jax.random.split(key, 4)
        inp = jax.random.normal(k1, (N, IN_F), jnp.float32)
        adj = jax.random.randint(k2, (N, N), 0, 2, jnp.int32)
        W = _xavier(k3, (IN_F, OUT_F))
        a = _xavier(k4, (2 * OUT_F, 1))
        return {'inp': inp, 'adj': adj, 'W': W, 'a': a}
    _L0_gnn_all = _L0_gnn_setup()
    _L0_gnn_in = {k: v for k, v in _L0_gnn_all.items() if k in ('W', 'a')}
    del _L0_gnn_all
    return {'x': x, 'adj': adj, 'L0_gnn_W': _L0_gnn_in['W'], 'L0_gnn_a': _L0_gnn_in['a']}

def reference(x, adj, L0_gnn_W, L0_gnn_a):
    import jax
    import jax.numpy as jnp

    def _L0_gnn_ref(inp, adj, W, a):
        import jax, jax.numpy as jnp
        import numpy as np
        N = 4096
        IN_F = 128
        OUT_F = 128
        ALPHA = 0.2
        NEG_INF = -1000000000000.0

        def _xavier(key, shape, gain=1.414):
            fan_in, fan_out = (shape[0], shape[1])
            bound = gain * np.sqrt(6.0 / (fan_in + fan_out))
            return jax.random.uniform(key, shape, jnp.float32, -bound, bound)
        h = inp @ W
        a1 = a[:OUT_F, 0]
        a2 = a[OUT_F:, 0]
        s1 = h @ a1
        s2 = h @ a2
        e = jax.nn.leaky_relu(s1[:, None] + s2[None, :], negative_slope=ALPHA)
        att = jnp.where(adj > 0, e, NEG_INF)
        att = jax.nn.softmax(att, axis=1)
        h_prime = att @ h
        return jax.nn.elu(h_prime)
    x = _layernorm(x + _L0_gnn_ref(x, adj, L0_gnn_W, L0_gnn_a), axis=-1)
    return x

_drawn_inputs = setup_inputs


def setup_inputs(seed=0):
    import zlib

    import numpy as np

    out = dict(_drawn_inputs(seed))
    spreads = {}
    factors = {}
    for name, (base, spread) in spreads.items():
        noise = np.random.default_rng([zlib.crc32(name.encode()), seed]).standard_normal(out[name].shape)
        drawn = base * np.exp(spread * noise) if base else spread * noise
        out[name] = jnp.asarray(drawn.astype(out[name].dtype))
    for name, factor in factors.items():
        out[name] = (out[name] * factor).astype(out[name].dtype)
    return out
```

```python
from contextlib import ExitStack

import numpy as np
import concourse.bass as bass
from concourse import mybir

F32 = mybir.dt.float32
BF16 = mybir.dt.bfloat16
I32 = mybir.dt.int32
ALU = mybir.AluOpType
ACT = mybir.ActivationFunctionType
AX = mybir.AxisListType

P = 128
N = 4096
TILES = 8
ROWS = TILES * P
CHUNKS = N // ROWS
STEPS = N // P
PAIR = 2
UNITS = STEPS // PAIR
ADJ_RING = 4
BODY = ADJ_RING
TURNS = UNITS // BODY
MASK_RING = 2
P_RING = 4
YW = P + 1
YS = 132
BANK = 512
SLOT = 256

ALPHA = 0.2
LIFT = 60.0
CUT = float(np.exp(np.float64(LIFT + 1.0)))
STEEP = 1.0e6
EPS = 1e-5


def gat_layer(nc, x_rows, x_cols, w_rows, w_cols, a_cols, identity, adj, out):
    with ExitStack() as ctx:
        def sb(name, shape, dt=F32):
            return ctx.enter_context(nc.sbuf_tensor(name, shape, dt))

        def sem(name):
            return ctx.enter_context(nc.semaphore(name))

        xT = sb("xT", [P, N])
        w_ext = sb("w_ext", [P, YW])
        wT = sb("wT", [P, P])
        a_sb = sb("a_sb", [P, 2])
        ident = sb("ident", [P, P])
        ones_row = sb("ones_row", [1, P])
        ones_sq = sb("ones_sq", [P, P])
        wa = sb("wa", [P, 2])
        wa1_wide = sb("wa1_wide", [P, P])
        x_sum = sb("x_sum", [P, 1])
        x_sum_wide = sb("x_sum_wide", [P, P])
        s2 = sb("s2", [P, STEPS])
        part_max = sb("part_max", [P, 1])
        top_one = sb("top_one", [1, 1])
        q_bias = sb("q_bias", [P, 1])
        f_bias = sb("f_bias", [P, 1])
        q = sb("q", [P, STEPS])
        f = sb("f", [P, STEPS])
        r = sb("r", [P, N])
        h_sum = sb("h_sum", [P, P])
        y = sb("y", [P, STEPS * YS])
        adj_ring = sb("adj_ring", [P, ADJ_RING, PAIR, ROWS], I32)
        mask_ring = sb("mask_ring", [P, MASK_RING, PAIR, ROWS], BF16)
        p_ring = sb("p_ring", [P, P_RING, ROWS])
        x_sb = sb("x_sb", [P, 2, ROWS])
        empty = sb("empty", [P, TILES])
        total = sb("total", [P, TILES])
        scale = sb("scale", [P, TILES])
        num = sb("num", [P, ROWS])
        exp_h = sb("exp_h", [P, ROWS])
        relu_h = sb("relu_h", [P, ROWS])
        elu_h = sb("elu_h", [P, ROWS])
        resid = sb("resid", [P, ROWS])
        stats = sb("stats", [P, TILES, 6])
        moments = sb("moments", [P, TILES, 2])
        eps_col = sb("eps_col", [P, 1])
        sigm_bias = sb("sigm_bias", [P, 1])
        std = sb("std", [P, TILES])
        rstd = sb("rstd", [P, TILES])
        res = sb("res", [P, 2, ROWS])

        ps = ctx.enter_context(nc.psum_tensor("ps", [P, 8 * BANK], F32))

        def acc(chunk):
            half = (chunk % 2) * 4 * BANK
            return ps[:, half:half + 4 * BANK].rearrange("p (n c) -> p n c", c=SLOT)

        y3 = y[:, :].rearrange("p (t c) -> p t c", c=YS)

        SPARE = 4 * BANK + YW + 3
        wa_ps = ps[:, SPARE:SPARE + 2]
        s2_ps = ps[:, SPARE + SLOT:SPARE + SLOT + STEPS]
        max_ps = ps[0:1, 0:P]
        top_ps = ps[:, BANK:BANK + 1]
        hsum_ps = ps[:, 2 * BANK:2 * BANK + P]

        w_landed = sem("w_landed")
        xT_landed = [sem(f"xT_landed{c}") for c in range(CHUNKS)]
        adj_landed = [sem(f"adj_landed{s}") for s in range(ADJ_RING)]
        x_landed = [sem("x_landed0"), sem("x_landed1")]
        stored = [sem("stored0"), sem("stored1")]
        consts_set = sem("consts_set")
        wa_summed = sem("wa_summed")
        wa_copied = sem("wa_copied")
        wa_spread = sem("wa_spread")
        xsum_done = sem("xsum_done")
        xsum_spread = sem("xsum_spread")
        s2_summed = sem("s2_summed")
        s2_copied = sem("s2_copied")
        part_max_done = sem("part_max_done")
        max_turned = sem("max_turned")
        top_found = sem("top_found")
        top_spread = sem("top_spread")
        bias_ready = sem("bias_ready")
        qf_ready = sem("qf_ready")
        s1_summed = sem("s1_summed")
        r_raw = sem("r_raw")
        r_ready = sem("r_ready")
        hsum_summed = sem("hsum_summed")
        hsum_copied = sem("hsum_copied")
        h_summed = sem("h_summed")
        y_ready = sem("y_ready")
        mask_ready = sem("mask_ready")
        p_ready = sem("p_ready")
        p_used = sem("p_used")
        empty_found = sem("empty_found")
        total_done = sem("total_done")
        scale_ready = sem("scale_ready")
        num_ready = sem("num_ready")
        exp_ready = sem("exp_ready")
        relu_ready = sem("relu_ready")
        elu_ready = sem("elu_ready")
        resid_ready = sem("resid_ready")
        stats_ready = sem("stats_ready")
        moments_ready = sem("moments_ready")
        std_ready = sem("std_ready")
        rstd_ready = sem("rstd_ready")
        res_ready = sem("res_ready")

        block = ctx.enter_context(nc.Block())

        @block.sync
        def _(sp):
            sp.dma_start(wT[:], w_cols).then_inc(w_landed, 16)
            sp.dma_start(a_sb[:], a_cols).then_inc(w_landed, 16)
            sp.dma_start(w_ext[:, 0:P], w_rows).then_inc(w_landed, 16)
            sp.dma_start(ident[:], identity).then_inc(w_landed, 16)
            for c in range(CHUNKS):
                sp.dma_start(xT[:, c * ROWS:(c + 1) * ROWS], x_cols[:, c * ROWS:(c + 1) * ROWS]).then_inc(xT_landed[c], 16)
            for s in range(ADJ_RING):
                sp.dma_start(adj_ring[:, s], adj[s]).then_inc(adj_landed[s], 16)

            with sp.Fori(1, CHUNKS * TURNS) as turn:
                for s in range(BODY):
                    sp.wait_ge(mask_ready, turn * BODY + (s - ADJ_RING + 1))
                    sp.dma_start(adj_ring[:, s], adj[bass.ds(turn * BODY + s, 1)].rearrange("u p k i -> p (u k) i")
                                 ).then_inc(adj_landed[s], 16)

        @block.gpsimd
        def _(pool):
            for c in range(2):
                pool.dma_start(x_sb[:, c], x_rows[c]).then_inc(x_landed[c], 16)
            for c in range(CHUNKS):
                pool.wait_ge(elu_ready, c + 1)
                pool.wait_ge(x_landed[c % 2], 16 * (c // 2 + 1))
                if c >= 1:
                    pool.wait_ge(res_ready, c)
                nc.gpsimd.tensor_tensor(resid[:], elu_h[:], x_sb[:, c % 2], ALU.add).then_inc(resid_ready, 1)
                if c + 2 < CHUNKS:
                    pool.wait_ge(resid_ready, c + 1)
                    pool.dma_start(x_sb[:, c % 2], x_rows[c + 2]).then_inc(x_landed[c % 2], 16)
                pool.wait_ge(res_ready, c + 1)
                pool.dma_start(out[c], res[:, c % 2]).then_inc(stored[c % 2], 16)
            for s in range(2):
                pool.wait_ge(stored[s], 16 * (CHUNKS // 2))

        @block.scalar
        def _(act):
            act.wait_ge(consts_set, 1)
            act.wait_ge(s2_copied, 1)
            act.wait_ge(bias_ready, 2)
            nc.scalar.activation(q[:], s2[:], ACT.Exp, bias=q_bias[:], scale=1.0 - ALPHA).then_inc(qf_ready, 1)
            nc.scalar.activation(f[:], s2[:], ACT.Exp, bias=f_bias[:], scale=ALPHA).then_inc(qf_ready, 1)
            for c in range(CHUNKS):
                act.wait_ge(s1_summed, c + 1)
                nc.scalar.activation(r[:, c * ROWS:(c + 1) * ROWS], ps[:, (c % 2) * 2 * BANK:(c % 2 + 1) * 2 * BANK], ACT.Exp,
                                     bias=q_bias[:], scale=-(1.0 - ALPHA)).then_inc(r_raw, 1)

            def mask(unit, s, landed):
                act.wait_ge(adj_landed[s], landed)
                nc.scalar.activation(mask_ring[:, s % MASK_RING], adj_ring[:, s], ACT.Sigmoid,
                                     bias=sigm_bias[:], scale=STEEP).then_inc(mask_ready, 1)

            def elu_parts(c):
                act.wait_ge(scale_ready, c + 1)
                act.wait_ge(num_ready, c + 1)
                if c >= 1:
                    act.wait_ge(elu_ready, c)
                for n in range(TILES):
                    cols = slice(n * P, (n + 1) * P)
                    e = nc.scalar.activation(exp_h[:, cols], num[:, cols], ACT.Exp, scale=scale[:, n:n + 1])
                e.then_inc(exp_ready, 1)
                for n in range(TILES):
                    cols = slice(n * P, (n + 1) * P)
                    e = nc.scalar.activation(relu_h[:, cols], num[:, cols], ACT.Relu, scale=scale[:, n:n + 1])
                e.then_inc(relu_ready, 1)

            def deviation(c):
                act.wait_ge(moments_ready, c + 1)
                nc.scalar.activation(std[:], moments[:, :, 1], ACT.Sqrt, bias=eps_col[:]).then_inc(std_ready, 1)

            for c in range(CHUNKS):
                for s in range(BODY):
                    unit = c * UNITS + s
                    if unit >= MASK_RING:
                        act.wait_ge(p_ready, PAIR * (unit - MASK_RING + 1))
                    mask(unit, s, 16 * (c * TURNS + 1))
                    if c >= 1 and s == 0:
                        elu_parts(c - 1)
                    if c >= 1 and s == 2:
                        deviation(c - 1)
                with act.Fori(c * TURNS + 1, (c + 1) * TURNS) as turn:
                    for s in range(BODY):
                        act.wait_ge(p_ready, turn * (PAIR * BODY) + PAIR * (s - MASK_RING + 1))
                        mask(None, s, turn * 16 + 16)
            elu_parts(CHUNKS - 1)
            deviation(CHUNKS - 1)

        @block.vector
        def _(dve):
            nc.vector.memset(ones_row[:], 1.0)
            nc.vector.memset(ones_sq[:], 1.0)
            nc.vector.memset(sigm_bias[:], -0.5 * STEEP)
            nc.vector.memset(eps_col[:], EPS).then_inc(consts_set, 1)
            dve.wait_ge(wa_summed, 1)
            nc.vector.tensor_copy(wa[:], wa_ps).then_inc(wa_copied, 1)
            dve.wait_ge(wa_copied, 1)
            dve.wait_ge(consts_set, 1)
            nc.vector.tensor_scalar(wa1_wide[:], ones_sq[:], wa[:, 0:1], None, ALU.mult).then_inc(wa_spread, 1)
            dve.wait_ge(w_landed, 64)
            nc.vector.tensor_copy(w_ext[:, P:YW], wa[:, 1:2]).then_inc(wa_spread, 1)
            for c in range(CHUNKS):
                dve.wait_ge(xT_landed[c], 16)
            nc.vector.reduce_sum(x_sum[:], xT[:], AX.X).then_inc(xsum_done, 1)
            dve.wait_ge(xsum_done, 1)
            nc.vector.tensor_scalar(x_sum_wide[:], ones_sq[:], x_sum[:, 0:1], None, ALU.mult).then_inc(xsum_spread, 1)
            dve.wait_ge(s2_summed, 1)
            nc.vector.reduce_max(part_max[:], s2_ps, AX.X).then_inc(part_max_done, 1)
            nc.vector.tensor_copy(s2[:], s2_ps).then_inc(s2_copied, 1)
            dve.wait_ge(max_turned, 1)
            nc.vector.reduce_max(top_one[:], max_ps, AX.X).then_inc(top_found, 1)
            dve.wait_ge(top_spread, 1)
            nc.vector.tensor_scalar(q_bias[:], top_ps, -(1.0 - ALPHA), LIFT, ALU.mult, ALU.add).then_inc(bias_ready, 1)
            nc.vector.tensor_scalar(f_bias[:], top_ps, -ALPHA, None, ALU.mult).then_inc(bias_ready, 1)
            dve.wait_ge(hsum_summed, 1)
            nc.vector.tensor_copy(h_sum[:], hsum_ps).then_inc(hsum_copied, 1)

            def cut_r(c):
                cols = r[:, c * ROWS:(c + 1) * ROWS]
                dve.wait_ge(r_raw, c + 1)
                nc.vector.tensor_scalar(cols, cols, CUT, None, ALU.min).then_inc(r_ready, 1)

            def make_y(c):
                t = slice(c * TILES, (c + 1) * TILES)
                dve.wait_ge(h_summed, c + 1)
                dve.wait_ge(qf_ready, 2)
                nc.vector.tensor_tensor(y3[:, t, 0:P], acc(1)[:, :, 0:P],
                                        f[:, t].unsqueeze(2).broadcast_to([P, TILES, P]), ALU.mult).then_inc(y_ready, 1)
                nc.vector.tensor_copy(y3[:, t, P], f[:, t]).then_inc(y_ready, 1)

            cut_r(0)
            make_y(0)

            def weigh(rows, k, q_col):
                slot = k % P_RING
                m = mask_ring[:, (k // PAIR) % MASK_RING, k % PAIR]
                nc.vector.scalar_tensor_tensor(p_ring[:, slot], rows, q_col, m, ALU.max, ALU.mult).then_inc(p_ready, 1)

            def totals(c):
                a = acc(c)
                dve.wait_ge(p_used, (c + 1) * STEPS)
                nc.vector.tensor_scalar(empty[:], a[:, :, P], 0.0, None, ALU.is_equal).then_inc(empty_found, 1)
                dve.wait_ge(empty_found, c + 1)
                nc.vector.scalar_tensor_tensor(total[:], empty[:], float(N), a[:, :, P], ALU.mult, ALU.add).then_inc(total_done, 1)
                dve.wait_ge(total_done, c + 1)
                nc.vector.reciprocal(scale[:], total[:]).then_inc(scale_ready, 1)
                dve.wait_ge(hsum_copied, 1)
                if c >= 1:
                    dve.wait_ge(relu_ready, c)
                for n in range(TILES):
                    u = nc.vector.scalar_tensor_tensor(num[:, n * P:(n + 1) * P], h_sum[:], empty[:, n:n + 1], a[:, n, 0:P],
                                                       ALU.mult, ALU.add)
                u.then_inc(num_ready, 1)

            def elu(c):
                dve.wait_ge(exp_ready, c + 1)
                dve.wait_ge(relu_ready, c + 1)
                if c >= 1:
                    dve.wait_ge(resid_ready, c)
                nc.vector.scalar_tensor_tensor(elu_h[:], exp_h[:], 1.0, relu_h[:], ALU.min, ALU.add).then_inc(elu_ready, 1)

            def row_moments(c):
                dve.wait_ge(resid_ready, c + 1)
                for n in range(TILES):
                    u = nc.vector.bn_stats(stats[:, n], resid[:, n * P:(n + 1) * P])
                u.then_inc(stats_ready, 1)
                dve.wait_ge(stats_ready, c + 1)
                for n in range(TILES):
                    u = nc.vector.bn_aggr(moments[:, n], stats[:, n])
                u.then_inc(moments_ready, 1)

            def normalise(c):
                dve.wait_ge(std_ready, c + 1)
                nc.vector.reciprocal(rstd[:], std[:]).then_inc(rstd_ready, 1)
                dve.wait_ge(rstd_ready, c + 1)
                if c >= 2:
                    dve.wait_ge(stored[c % 2], 16 * (c // 2))
                for n in range(TILES):
                    cols = slice(n * P, (n + 1) * P)
                    u = nc.vector.tensor_scalar(res[:, c % 2, cols], resid[:, cols], moments[:, n, 0:1], rstd[:, n:n + 1],
                                                ALU.subtract, ALU.mult)
                u.then_inc(res_ready, 1)

            for c in range(CHUNKS):
                rows = r[:, c * ROWS:(c + 1) * ROWS]
                dve.wait_ge(r_ready, c + 1)
                for k in range(PAIR * BODY):
                    step = c * STEPS + k
                    if k % PAIR == 0:
                        dve.wait_ge(mask_ready, step // PAIR + 1)
                    if step >= P_RING:
                        dve.wait_ge(p_used, step - P_RING + 1)
                    weigh(rows, k, q[:, k:k + 1])
                    if c == 0 and k in (1, 3, 5):
                        make_y((k + 1) // 2)
                        cut_r((k + 1) // 2)
                    if c >= 1 and k == 0:
                        totals(c - 1)
                    if c >= 1 and k == 3:
                        elu(c - 1)
                    if c >= 1 and k == 4:
                        row_moments(c - 1)
                    if c >= 1 and k == 7:
                        normalise(c - 1)
                with dve.Fori(1, TURNS) as turn:
                    for k in range(PAIR * BODY):
                        if k % PAIR == 0:
                            dve.wait_ge(mask_ready, turn * BODY + (c * UNITS + k // PAIR + 1))
                        dve.wait_ge(p_used, turn * (PAIR * BODY) + (c * STEPS + k - P_RING + 1))
                        weigh(rows, k, q[:, bass.ds(turn * (PAIR * BODY) + k, 1)])
            c = CHUNKS - 1
            totals(c)
            elu(c)
            row_moments(c)
            normalise(c)

        @block.tensor
        def _(pe):
            pe.wait_ge(w_landed, 64)
            nc.tensor.matmul(wa_ps, wT[:], a_sb[:], start=True, stop=True).then_inc(wa_summed, 1)
            pe.wait_ge(wa_copied, 1)
            for t in range(STEPS):
                if t % TILES == 0:
                    pe.wait_ge(xT_landed[t // TILES], 16)
                m = nc.tensor.matmul(s2_ps[:, t:t + 1], xT[:, t * P:(t + 1) * P], wa[:, 1:2], start=True, stop=True)
            m.then_inc(s2_summed, 1)
            pe.wait_ge(part_max_done, 1)
            nc.tensor.transpose(max_ps, part_max[:], ident[:]).then_inc(max_turned, 1)
            pe.wait_ge(xsum_spread, 1)
            nc.tensor.matmul(hsum_ps, x_sum_wide[:], w_ext[:, 0:P], start=True, stop=True).then_inc(hsum_summed, 1)
            pe.wait_ge(top_found, 1)
            nc.tensor.matmul(top_ps, ones_row[:], top_one[:], start=True, stop=True).then_inc(top_spread, 1)
            pe.wait_ge(wa_spread, 2)

            def s1_rows(c):
                for half in range(2):
                    cols = slice(c * ROWS + half * BANK, c * ROWS + (half + 1) * BANK)
                    bank = (c % 2) * 2 + half
                    m = nc.tensor.matmul(ps[:, bank * BANK:(bank + 1) * BANK], wa1_wide[:], xT[:, cols], start=True, stop=True)
                m.then_inc(s1_summed, 1)

            def h_tiles(c):
                for n in range(TILES):
                    t = c * TILES + n
                    m = nc.tensor.matmul(acc(1)[:, n, 0:P], xT[:, t * P:(t + 1) * P], w_ext[:, 0:P], start=True, stop=True)
                m.then_inc(h_summed, 1)

            pe.wait_ge(bias_ready, 2)
            pe.wait_ge(s2_copied, 1)
            s1_rows(0)
            h_tiles(0)
            pe.wait_ge(hsum_copied, 1)
            s1_rows(1)
            for c in (2, 3):
                pe.wait_ge(r_raw, c - 1)
                s1_rows(c)
            pe.wait_ge(r_raw, CHUNKS)

            def add_up(c, k, y_tile, first):
                for n in range(TILES):
                    m = nc.tensor.matmul(acc(c)[:, n, 0:YW], p_ring[:, k % P_RING, n * P:(n + 1) * P], y_tile,
                                         start=(first and n % 2 == 0), stop=True, skip_group_check=True)
                m.then_inc(p_used, 1)

            for c in range(CHUNKS):
                if c >= 2:
                    pe.wait_ge(num_ready, c - 1)
                for k in range(PAIR * BODY):
                    if c == 0 and k == 0:
                        pe.wait_ge(y_ready, 2)
                    pe.wait_ge(p_ready, c * STEPS + k + 1)
                    add_up(c, k, y3[:, k, 0:YW], k == 0)
                    if c == 0 and k in (0, 2, 4):
                        pe.wait_ge(y_ready, k + 2)
                        h_tiles(k // 2 + 1)
                if c == 0:
                    pe.wait_ge(y_ready, 2 * CHUNKS)
                with pe.Fori(1, TURNS) as turn:
                    for k in range(PAIR * BODY):
                        pe.wait_ge(p_ready, turn * (PAIR * BODY) + (c * STEPS + k + 1))
                        add_up(c, k, y[:, bass.ds(turn * (PAIR * BODY * YS) + k * YS, YW)], False)


def kernel(x, adj, L0_gnn_W, L0_gnn_a):
    import concourse.bacc as bacc
    from concourse.bass_utils import run_bass_kernel_spmd

    x, adj, W, a = (np.asarray(v) for v in (x, adj, L0_gnn_W, L0_gnn_a))
    v = adj.reshape(CHUNKS, P, TILES, CHUNKS, P, TILES // PAIR, PAIR)
    v = np.ascontiguousarray(v.transpose(0, 3, 5, 4, 6, 2, 1)).reshape(CHUNKS * UNITS, P, PAIR, ROWS)
    arrays = {
        "x_rows": x.reshape(CHUNKS, P, ROWS),
        "x_cols": np.ascontiguousarray(x.reshape(CHUNKS, P, TILES, P).transpose(3, 0, 2, 1)).reshape(P, N),
        "w_rows": W,
        "w_cols": np.ascontiguousarray(W.T),
        "a_cols": np.ascontiguousarray(a.reshape(2, P).T),
        "identity": np.eye(P, dtype=np.float32),
        "adj": v,
    }
    nc = bacc.Bacc("TRN2", target_bir_lowering=False, num_devices=1)
    aps = [nc.dram_tensor(n, list(v.shape), mybir.dt.from_np(v.dtype), kind="ExternalInput").ap() for n, v in arrays.items()]
    out = nc.dram_tensor("out", [CHUNKS, P, ROWS], F32, kind="ExternalOutput").ap()
    gat_layer(nc, *aps, out)
    result = run_bass_kernel_spmd(nc, [arrays], core_ids=[0])
    return result.results[0]["out"].reshape(N, P)
```

```python
from contextlib import ExitStack

import numpy as np
import concourse.bass as bass
from concourse import mybir

F32 = mybir.dt.float32
BF16 = mybir.dt.bfloat16
I32 = mybir.dt.int32
ALU = mybir.AluOpType
ACT = mybir.ActivationFunctionType
AX = mybir.AxisListType

P = 128
N = 4096
TILES = 8
ROWS = TILES * P
CHUNKS = N // ROWS
STEPS = N // P
PAIR = 2
UNITS = STEPS // PAIR
ADJ_RING = 4
BODY = ADJ_RING
TURNS = UNITS // BODY
MASK_RING = BODY
P_RING = PAIR * BODY
GROUP = 2
GROUPS = TILES // GROUP
GROUPED = 4
H_AT = [0, 3, 5]
Y_AT = [2, 5, 7]
TOTALS_AT = 7
YW = P + 1
YS = 132
BANK = 512
SLOT = 256

ALPHA = 0.2
LIFT = 60.0
CUT = float(np.exp(np.float64(LIFT + 1.0)))
STEEP = 1.0e6
EPS = 1e-5


def gat_layer(nc, x_rows, x_cols, packed, adj, out):
    with ExitStack() as ctx:
        def sb(name, shape, dt=F32):
            return ctx.enter_context(nc.sbuf_tensor(name, shape, dt))

        def sem(name):
            return ctx.enter_context(nc.semaphore(name))

        xT = sb("xT", [P, N])
        weights = sb("weights", [P, 3 * P + 2])
        wT, a_sb = weights[:, 0:P], weights[:, P:P + 2]
        w_sb, ident = weights[:, P + 2:2 * P + 2], weights[:, 2 * P + 2:3 * P + 2]
        ones_row = sb("ones_row", [1, P])
        ones_sq = sb("ones_sq", [P, P])
        wa = sb("wa", [P, 2])
        wa1_wide = sb("wa1_wide", [P, P])
        halves = sb("halves", [P, N // 2])
        table_junk = sb("table_junk", [P, 1])
        x_sum_wide = sb("x_sum_wide", [P, P])
        part_max = sb("part_max", [P, 1])
        top_one = sb("top_one", [1, 1])
        q_bias = sb("q_bias", [P, 1])
        f_bias = sb("f_bias", [P, 1])
        q = sb("q", [P, STEPS])
        f = sb("f", [P, STEPS])
        r = sb("r", [P, N])
        h_sum = sb("h_sum", [P, P])
        y = sb("y", [P, STEPS * YS])
        adj_ring = sb("adj_ring", [P, ADJ_RING, PAIR, ROWS], I32)
        mask_ring = sb("mask_ring", [P, MASK_RING, PAIR, ROWS], BF16)
        p_ring = sb("p_ring", [P, P_RING, ROWS])
        x_sb = sb("x_sb", [P, 2, ROWS])
        empty = sb("empty", [P, TILES])
        total = sb("total", [P, TILES])
        scale = sb("scale", [P, TILES])
        num = sb("num", [P, ROWS])
        exp_h = sb("exp_h", [P, ROWS])
        relu_h = sb("relu_h", [P, ROWS])
        elu_h = sb("elu_h", [P, ROWS])
        resid = sb("resid", [P, ROWS])
        stats = sb("stats", [P, TILES, 6])
        moments = sb("moments", [P, TILES, 2])
        eps_col = sb("eps_col", [P, 1])
        sigm_bias = sb("sigm_bias", [P, 1])
        std = sb("std", [P, TILES])
        rstd = sb("rstd", [P, TILES])
        res = sb("res", [P, 2, ROWS])

        ps = ctx.enter_context(nc.psum_tensor("ps", [P, 8 * BANK], F32))

        def acc(chunk):
            half = (chunk % 2) * 4 * BANK
            return ps[:, half:half + 4 * BANK].rearrange("p (n c) -> p n c", c=SLOT)

        def s1_ps(chunk):
            bank = 4 + 2 * (chunk % 2)
            return ps[:, bank * BANK:(bank + 2) * BANK]

        y3 = y[:, :].rearrange("p (t c) -> p t c", c=YS)

        last_bank = ps[:, 7 * BANK:8 * BANK]
        s2_ps = last_bank[:, 0:STEPS]
        wa_ps = last_bank[:, STEPS:STEPS + 2]
        top_ps = last_bank[:, STEPS + 2:STEPS + 3]
        max_ps = last_bank[0:1, P:2 * P]
        hsum_ps = acc(1)[:, 0, P:2 * P]

        w_landed = sem("w_landed")
        xT_landed = [sem(f"xT_landed{c}") for c in range(CHUNKS)]
        adj_landed = [sem(f"adj_landed{s}") for s in range(ADJ_RING)]
        x_landed = [sem("x_landed0"), sem("x_landed1")]
        stored = [sem("stored0"), sem("stored1")]
        last_stored = sem("last_stored")
        consts_set = sem("consts_set")
        wa_summed = sem("wa_summed")
        wa_copied = sem("wa_copied")
        wa1_spread = sem("wa1_spread")
        xsum_done = sem("xsum_done")
        xsum_spread = sem("xsum_spread")
        s2_summed = sem("s2_summed")
        part_max_done = sem("part_max_done")
        max_turned = sem("max_turned")
        top_found = sem("top_found")
        top_spread = sem("top_spread")
        bias_ready = sem("bias_ready")
        qf_ready = sem("qf_ready")
        s1_summed = sem("s1_summed")
        r_raw = sem("r_raw")
        r_ready = sem("r_ready")
        hsum_summed = sem("hsum_summed")
        hsum_copied = sem("hsum_copied")
        h_summed = sem("h_summed")
        y_ready = sem("y_ready")
        first_mask = sem("first_mask")
        mask_ready = sem("mask_ready")
        p_ready = sem("p_ready")
        p_used = sem("p_used")
        last_sums = sem("last_sums")
        empty_found = sem("empty_found")
        total_done = sem("total_done")
        scale_ready = sem("scale_ready")
        num_ready = sem("num_ready")
        exp_ready = sem("exp_ready")
        relu_ready = sem("relu_ready")
        elu_ready = sem("elu_ready")
        resid_ready = sem("resid_ready")
        last_resid = sem("last_resid")
        stats_ready = sem("stats_ready")
        moments_ready = sem("moments_ready")
        std_ready = sem("std_ready")
        rstd_ready = sem("rstd_ready")
        res_ready = sem("res_ready")
        last_res_ready = sem("last_res_ready")

        block = ctx.enter_context(nc.Block())

        @block.sync
        def _(sp):
            sp.dma_start(weights[:], packed).then_inc(w_landed, 16)
            for c in range(CHUNKS):
                sp.dma_start(xT[:, c * ROWS:(c + 1) * ROWS], x_cols[:, c * ROWS:(c + 1) * ROWS]).then_inc(xT_landed[c], 16)
            for s in range(ADJ_RING):
                if s < 2:
                    sp.wait_ge(xT_landed[2 * s + 1], 16)
                sp.dma_start(adj_ring[:, s], adj[s]).then_inc(adj_landed[s], 16)
            with sp.Fori(1, CHUNKS * TURNS) as turn:
                for s in range(BODY):
                    sp.wait_ge(mask_ready, turn * BODY + (s - ADJ_RING + 1))
                    sp.dma_start(adj_ring[:, s], adj[bass.ds(turn * BODY + s, 1)].rearrange("u p k i -> p (u k) i")
                                 ).then_inc(adj_landed[s], 16)
            for half in range(2):
                cols = slice(half * ROWS // 2, (half + 1) * ROWS // 2)
                sp.wait_ge(last_res_ready, half + 1)
                sp.dma_start(out[CHUNKS - 1][:, cols], res[:, (CHUNKS - 1) % 2, cols]).then_inc(last_stored, 16)
            sp.wait_ge(last_stored, 32)

        @block.gpsimd
        def _(pool):
            for c in range(2):
                pool.dma_start(x_sb[:, c], x_rows[c]).then_inc(x_landed[c], 16)
            for c in range(CHUNKS):
                pool.wait_ge(xT_landed[c], 16)
            width = N // 2
            nc.gpsimd.tensor_tensor(halves[:, 0:width], xT[:, 0:width], xT[:, width:N], ALU.add).then_inc(xsum_done, 1)
            folds = 1
            while width > 1:
                width //= 2
                pool.wait_ge(xsum_done, folds)
                nc.gpsimd.tensor_tensor(halves[:, 0:width], halves[:, 0:width], halves[:, width:2 * width], ALU.add
                                        ).then_inc(xsum_done, 1)
                folds += 1
            pool.wait_ge(xsum_done, folds)
            pool.wait_ge(consts_set, 1)
            nc.gpsimd.tensor_scalar(x_sum_wide[:], ones_sq[:], halves[:, 0:1], None, ALU.mult).then_inc(xsum_spread, 1)

            for c in range(CHUNKS - 1):
                pool.wait_ge(elu_ready, c + 1)
                pool.wait_ge(x_landed[c % 2], 16 * (c // 2 + 1))
                if c >= 1:
                    pool.wait_ge(res_ready, c)
                nc.gpsimd.tensor_tensor(resid[:], elu_h[:], x_sb[:, c % 2], ALU.add).then_inc(resid_ready, 1)
                if c + 2 < CHUNKS:
                    pool.wait_ge(resid_ready, c + 1)
                    pool.dma_start(x_sb[:, c % 2], x_rows[c + 2]).then_inc(x_landed[c % 2], 16)
                pool.wait_ge(res_ready, c + 1)
                pool.dma_start(out[c], res[:, c % 2]).then_inc(stored[c % 2], 16)
            pool.wait_ge(stored[0], 32)
            pool.wait_ge(stored[1], 16)

        @block.scalar
        def _(act):
            act.wait_ge(consts_set, 1)
            nc.scalar.activation(table_junk[:], eps_col[:], ACT.Exp)

            act.wait_ge(bias_ready, 2)
            nc.scalar.activation(q[:], s2_ps, ACT.Exp, bias=q_bias[:], scale=1.0 - ALPHA).then_inc(qf_ready, 1)
            nc.scalar.activation(f[:], s2_ps, ACT.Exp, bias=f_bias[:], scale=ALPHA).then_inc(qf_ready, 1)

            def make_r(c):
                act.wait_ge(s1_summed, c + 1)
                nc.scalar.activation(r[:, c * ROWS:(c + 1) * ROWS], s1_ps(c), ACT.Exp,
                                     bias=q_bias[:], scale=-(1.0 - ALPHA)).then_inc(r_raw, 1)

            make_r(0)
            make_r(1)

            def mask(s, landed, count=1):
                act.wait_ge(adj_landed[s], landed)
                nc.scalar.activation(mask_ring[:, s], adj_ring[:, s], ACT.Sigmoid,
                                     bias=sigm_bias[:], scale=STEEP).then_inc(mask_ready, count)

            def elu_parts(g, before, tiles):
                act.wait_ge(scale_ready, g + 1)
                act.wait_ge(num_ready, g + 1)
                if before:
                    act.wait_ge(elu_ready, before)
                for n in tiles:
                    cols = slice(n * P, (n + 1) * P)
                    e = nc.scalar.activation(exp_h[:, cols], num[:, cols], ACT.Exp, scale=scale[:, n:n + 1])
                e.then_inc(exp_ready, 1)
                for n in tiles:
                    cols = slice(n * P, (n + 1) * P)
                    e = nc.scalar.activation(relu_h[:, cols], num[:, cols], ACT.Relu, scale=scale[:, n:n + 1])
                e.then_inc(relu_ready, 1)

            def deviation(c, groups):
                act.wait_ge(moments_ready, groups)
                nc.scalar.activation(std[:], moments[:, :, 1], ACT.Sqrt, bias=eps_col[:]).then_inc(std_ready, 1)

            for c in range(CHUNKS):
                for s in range(BODY):
                    unit = c * UNITS + s
                    if unit == 0:
                        act.wait_ge(first_mask, 1)
                        continue
                    if unit >= MASK_RING:
                        act.wait_ge(p_ready, PAIR * (unit - MASK_RING + 1))
                    mask(s, 16 * (c * TURNS + 1), 2 if unit == 1 else 1)

                def turn_of_masks(turn):
                    for s in range(BODY):
                        act.wait_ge(p_ready, turn * (PAIR * BODY) + PAIR * (s - MASK_RING + 1))
                        mask(s, turn * 16 + 16)

                if c >= 1:
                    elu_parts(c - 1, c - 1, range(TILES))
                    turn_of_masks(c * TURNS + 1)
                    deviation(c - 1, c)
                with act.Fori(c * TURNS + (2 if c >= 1 else 1), (c + 1) * TURNS) as turn:
                    turn_of_masks(turn)
                if c == 0:
                    make_r(2)
                    make_r(3)
            nc.scalar.activation(table_junk[:], eps_col[:], ACT.Exp)
            for g in range(GROUPS):
                elu_parts(CHUNKS - 1 + g, CHUNKS - 1, range(g * GROUP, (g + 1) * GROUP))
            nc.scalar.activation(table_junk[:], eps_col[:], ACT.Sqrt)
            deviation(CHUNKS - 1, CHUNKS - 1 + GROUPS)

        @block.vector
        def _(dve):
            nc.vector.memset(ones_row[:], 1.0)
            nc.vector.memset(ones_sq[:], 1.0)
            nc.vector.memset(sigm_bias[:], -0.5 * STEEP)
            nc.vector.memset(eps_col[:], EPS).then_inc(consts_set, 1)
            dve.wait_ge(wa_summed, 1)
            nc.vector.tensor_copy(wa[:], wa_ps).then_inc(wa_copied, 1)
            dve.wait_ge(wa_copied, 1)
            dve.wait_ge(consts_set, 1)
            nc.vector.tensor_scalar(wa1_wide[:], ones_sq[:], wa[:, 0:1], None, ALU.mult).then_inc(wa1_spread, 1)
            dve.wait_ge(s2_summed, 1)
            nc.vector.reduce_max(part_max[:], s2_ps, AX.X).then_inc(part_max_done, 1)
            dve.wait_ge(max_turned, 1)
            nc.vector.reduce_max(top_one[:], max_ps, AX.X).then_inc(top_found, 1)
            dve.wait_ge(top_spread, 1)
            nc.vector.tensor_scalar(q_bias[:], top_ps, -(1.0 - ALPHA), LIFT, ALU.mult, ALU.add).then_inc(bias_ready, 1)
            nc.vector.tensor_scalar(f_bias[:], top_ps, -ALPHA, None, ALU.mult).then_inc(bias_ready, 1)
            dve.wait_ge(adj_landed[0], 16)
            nc.vector.tensor_scalar(mask_ring[:, 0], adj_ring[:, 0], 0.0, None, ALU.is_gt).then_inc(first_mask, 1)

            def cut_r(c):
                cols = r[:, c * ROWS:(c + 1) * ROWS]
                dve.wait_ge(r_raw, c + 1)
                nc.vector.tensor_scalar(cols, cols, CUT, None, ALU.min).then_inc(r_ready, 1)

            def make_y(c):
                t = slice(c * TILES, (c + 1) * TILES)
                dve.wait_ge(h_summed, c + 1)
                dve.wait_ge(qf_ready, 2)
                nc.vector.tensor_tensor(y3[:, t, 0:P], acc(min(c, 1))[:, :, 0:P],
                                        f[:, t].unsqueeze(2).broadcast_to([P, TILES, P]), ALU.mult).then_inc(y_ready, 1)
                nc.vector.tensor_copy(y3[:, t, P], f[:, t]).then_inc(y_ready, 1)

            make_y(0)
            cut_r(0)

            def weigh(rows, k, q_col):
                m = mask_ring[:, (k // PAIR) % MASK_RING, k % PAIR]
                nc.vector.scalar_tensor_tensor(p_ring[:, k % P_RING], rows, q_col, m, ALU.max, ALU.mult).then_inc(p_ready, 1)

            def totals(c, g, before, tiles):
                a = acc(c)
                t = slice(tiles[0], tiles[-1] + 1)
                nc.vector.tensor_scalar(empty[:, t], a[:, t, P], 0.0, None, ALU.is_equal).then_inc(empty_found, 1)
                dve.wait_ge(empty_found, g + 1)
                nc.vector.scalar_tensor_tensor(total[:, t], empty[:, t], float(N), a[:, t, P], ALU.mult, ALU.add
                                               ).then_inc(total_done, 1)
                dve.wait_ge(total_done, g + 1)
                nc.vector.reciprocal(scale[:, t], total[:, t]).then_inc(scale_ready, 1)
                dve.wait_ge(hsum_copied, 1)
                if before:
                    dve.wait_ge(relu_ready, before)
                for n in tiles:
                    u = nc.vector.scalar_tensor_tensor(num[:, n * P:(n + 1) * P], h_sum[:], empty[:, n:n + 1], a[:, n, 0:P],
                                                       ALU.mult, ALU.add)
                u.then_inc(num_ready, 1)

            def elu(g, before, tiles):
                cols = slice(tiles[0] * P, (tiles[-1] + 1) * P)
                dve.wait_ge(exp_ready, g + 1)
                dve.wait_ge(relu_ready, g + 1)
                if before:
                    dve.wait_ge(resid_ready, before)
                nc.vector.scalar_tensor_tensor(elu_h[:, cols], exp_h[:, cols], 1.0, relu_h[:, cols], ALU.min, ALU.add
                                               ).then_inc(elu_ready, 1)

            def row_moments(g, tiles):
                for n in tiles:
                    u = nc.vector.bn_stats(stats[:, n], resid[:, n * P:(n + 1) * P])
                u.then_inc(stats_ready, 1)
                dve.wait_ge(stats_ready, g + 1)
                for n in tiles:
                    u = nc.vector.bn_aggr(moments[:, n], stats[:, n])
                u.then_inc(moments_ready, 1)

            def inverse_deviation(c):
                dve.wait_ge(std_ready, c + 1)
                nc.vector.reciprocal(rstd[:], std[:]).then_inc(rstd_ready, 1)
                dve.wait_ge(rstd_ready, c + 1)

            def normalise(c, tiles):
                for n in tiles:
                    cols = slice(n * P, (n + 1) * P)
                    u = nc.vector.tensor_scalar(res[:, c % 2, cols], resid[:, cols], moments[:, n, 0:1], rstd[:, n:n + 1],
                                                ALU.subtract, ALU.mult)
                return u

            for c in range(CHUNKS):
                rows = r[:, c * ROWS:(c + 1) * ROWS]
                dve.wait_ge(r_ready, c + 1)
                for k in range(PAIR * BODY):
                    step = c * STEPS + k
                    if step == 0:
                        dve.wait_ge(first_mask, 1)
                    elif step % PAIR == 0:
                        dve.wait_ge(mask_ready, step // PAIR + 1)
                    if step >= P_RING:
                        dve.wait_ge(p_used, step - P_RING + 1)
                    weigh(rows, k, q[:, k:k + 1])
                    if c == 0 and k in Y_AT:
                        make_y(Y_AT.index(k) + 1)
                    if c == 0 and k == 7:
                        dve.wait_ge(hsum_summed, 1)
                        nc.vector.tensor_copy(h_sum[:], hsum_ps).then_inc(hsum_copied, 1)
                        cut_r(1)
                    if c >= 1 and k == TOTALS_AT:
                        dve.wait_ge(p_used, c * STEPS)
                        totals(c - 1, c - 1, c - 1, range(TILES))

                def turn_of_steps(turn, between):
                    for k in range(PAIR * BODY):
                        if k % PAIR == 0:
                            dve.wait_ge(mask_ready, turn * BODY + (c * UNITS + k // PAIR + 1))
                        dve.wait_ge(p_used, turn * (PAIR * BODY) + (c * STEPS + k - P_RING + 1))
                        weigh(rows, k, q[:, bass.ds(turn * (PAIR * BODY) + k, 1)])
                        if between:
                            between(k)

                def last_stages(k):
                    if k == 1:
                        elu(c - 1, c - 1, range(TILES))
                    if k == 4:
                        dve.wait_ge(resid_ready, c)
                        row_moments(c - 1, range(TILES))
                    if k == 6:
                        inverse_deviation(c - 1)
                        if c - 1 >= 2:
                            dve.wait_ge(stored[(c - 1) % 2], 16 * ((c - 1) // 2))
                        normalise(c - 1, range(TILES)).then_inc(res_ready, 1)

                if c >= 1:
                    turn_of_steps(1, last_stages)
                with dve.Fori(2 if c >= 1 else 1, TURNS) as turn:
                    turn_of_steps(turn, None)
                if c == 0:
                    cut_r(2)
                    cut_r(3)

            c = CHUNKS - 1

            def last_moments(g):
                tiles = range(g * GROUP, (g + 1) * GROUP)
                cols = slice(g * GROUP * P, (g + 1) * GROUP * P)
                elu(c + g, c, tiles)
                dve.wait_ge(elu_ready, c + g + 1)
                nc.vector.tensor_tensor(resid[:, cols], elu_h[:, cols], x_sb[:, c % 2, cols], ALU.add).then_inc(last_resid, 1)
                dve.wait_ge(last_resid, g + 1)
                row_moments(c + g, tiles)

            dve.wait_ge(x_landed[c % 2], 32)
            for g in range(GROUPS):
                dve.wait_ge(last_sums, g + 1)
                totals(c, c + g, c, range(g * GROUP, (g + 1) * GROUP))
                if g >= 1:
                    last_moments(g - 1)
            last_moments(GROUPS - 1)
            inverse_deviation(c)
            dve.wait_ge(stored[c % 2], 16)
            for half in range(2):
                normalise(c, range(half * TILES // 2, (half + 1) * TILES // 2)).then_inc(last_res_ready, 1)

        @block.tensor
        def _(pe):
            pe.wait_ge(w_landed, 16)
            nc.tensor.matmul(wa_ps, wT, a_sb, start=True, stop=True).then_inc(wa_summed, 1)
            pe.wait_ge(wa_copied, 1)
            for t in range(STEPS):
                if t % TILES == 0:
                    pe.wait_ge(xT_landed[t // TILES], 16)
                m = nc.tensor.matmul(s2_ps[:, t:t + 1], xT[:, t * P:(t + 1) * P], wa[:, 1:2], start=True, stop=True)
            m.then_inc(s2_summed, 1)

            def s1_rows(c):
                for half in range(2):
                    cols = slice(c * ROWS + half * BANK, c * ROWS + (half + 1) * BANK)
                    m = nc.tensor.matmul(s1_ps(c)[:, half * BANK:(half + 1) * BANK], wa1_wide[:], xT[:, cols],
                                         start=True, stop=True)
                m.then_inc(s1_summed, 1)

            def h_tiles(c):
                for n in range(TILES):
                    t = c * TILES + n
                    m = nc.tensor.matmul(acc(min(c, 1))[:, n, 0:P], xT[:, t * P:(t + 1) * P], w_sb,
                                         start=True, stop=True)
                m.then_inc(h_summed, 1)

            pe.wait_ge(part_max_done, 1)
            nc.tensor.transpose(max_ps, part_max[:], ident).then_inc(max_turned, 1)
            pe.wait_ge(wa1_spread, 1)
            s1_rows(0)
            pe.wait_ge(consts_set, 1)
            pe.wait_ge(top_found, 1)
            nc.tensor.matmul(top_ps, ones_row[:], top_one[:], start=True, stop=True).then_inc(top_spread, 1)
            h_tiles(0)
            pe.wait_ge(qf_ready, 2)
            s1_rows(1)

            def add_up(c, k, tiles, y_tile, first):
                for n in tiles:
                    m = nc.tensor.matmul(acc(c)[:, n, 0:YW], p_ring[:, k % P_RING, n * P:(n + 1) * P], y_tile,
                                         start=(first and n % 2 == 0), stop=True, skip_group_check=True)
                return m

            for c in range(CHUNKS):
                if c == 1:
                    pe.wait_ge(r_raw, CHUNKS)
                if c >= 2:
                    pe.wait_ge(num_ready, c - 1)
                for k in range(PAIR * BODY):
                    if c == 0 and k == 0:
                        pe.wait_ge(y_ready, 2)
                    pe.wait_ge(p_ready, c * STEPS + k + 1)
                    add_up(c, k, range(TILES), y3[:, k, 0:YW], k == 0).then_inc(p_used, 1)
                    if c == 0 and k in H_AT:
                        nodes = H_AT.index(k) + 1
                        pe.wait_ge(r_raw, 2)
                        pe.wait_ge(y_ready, 2 * nodes)
                        if nodes == CHUNKS - 1:
                            pe.wait_ge(xsum_spread, 1)
                            nc.tensor.matmul(hsum_ps, x_sum_wide[:], w_sb, start=True, stop=True
                                             ).then_inc(hsum_summed, 1)
                        h_tiles(nodes)
                if c == 0:
                    pe.wait_ge(y_ready, 2 * CHUNKS)
                    pe.wait_ge(hsum_copied, 1)
                    s1_rows(2)
                    s1_rows(3)
                turns = TURNS - 1 if c == CHUNKS - 1 else TURNS
                with pe.Fori(1, turns) as turn:
                    for k in range(PAIR * BODY):
                        pe.wait_ge(p_ready, turn * (PAIR * BODY) + (c * STEPS + k + 1))
                        add_up(c, k, range(TILES), y[:, bass.ds(turn * (PAIR * BODY * YS) + k * YS, YW)], False
                               ).then_inc(p_used, 1)
            c = CHUNKS - 1
            for k in range(STEPS - PAIR * BODY, STEPS - GROUPED):
                pe.wait_ge(p_ready, c * STEPS + k + 1)
                add_up(c, k, range(TILES), y3[:, k, 0:YW], False).then_inc(p_used, 1)
            pe.wait_ge(p_ready, CHUNKS * STEPS)
            for g in range(GROUPS):
                for k in range(STEPS - GROUPED, STEPS):
                    m = add_up(c, k, range(g * GROUP, (g + 1) * GROUP), y3[:, k, 0:YW], False)
                m.then_inc(last_sums, 1)


def kernel(x, adj, L0_gnn_W, L0_gnn_a):
    import concourse.bacc as bacc
    from concourse.bass_utils import run_bass_kernel_spmd

    x, adj, W, a = (np.asarray(v) for v in (x, adj, L0_gnn_W, L0_gnn_a))
    v = adj.reshape(CHUNKS, P, TILES, CHUNKS, P, TILES // PAIR, PAIR)
    v = np.ascontiguousarray(v.transpose(0, 3, 5, 4, 6, 2, 1)).reshape(CHUNKS * UNITS, P, PAIR, ROWS)
    arrays = {
        "x_rows": x.reshape(CHUNKS, P, ROWS),
        "x_cols": np.ascontiguousarray(x.reshape(CHUNKS, P, TILES, P).transpose(3, 0, 2, 1)).reshape(P, N),
        "packed": np.concatenate([W.T, a.reshape(2, P).T, W, np.eye(P, dtype=np.float32)], axis=1),
        "adj": v,
    }
    nc = bacc.Bacc("TRN2", target_bir_lowering=False, num_devices=1)
    aps = [nc.dram_tensor(n, list(v.shape), mybir.dt.from_np(v.dtype), kind="ExternalInput").ap() for n, v in arrays.items()]
    out = nc.dram_tensor("out", [CHUNKS, P, ROWS], F32, kind="ExternalOutput").ap()
    gat_layer(nc, *aps, out)
    result = run_bass_kernel_spmd(nc, [arrays], core_ids=[0])
    return result.results[0]["out"].reshape(N, P)
```

```python
from contextlib import ExitStack

import numpy as np
import concourse.bass as bass
from concourse import mybir

F32 = mybir.dt.float32
BF16 = mybir.dt.bfloat16
I32 = mybir.dt.int32
ALU = mybir.AluOpType
ACT = mybir.ActivationFunctionType
AX = mybir.AxisListType

P = 128
N = 4096
TILES = 8
ROWS = TILES * P
HALF = ROWS // 2
CHUNKS = N // ROWS
STEPS = N // P
PAIR = 2
UNITS = STEPS // PAIR
ADJ_RING = 4
BODY = ADJ_RING
TURNS = UNITS // BODY
MASK_RING = BODY
P_RING = PAIR * BODY
GROUP = 2
GROUPS = TILES // GROUP
GROUPED = 8
WARMING = 7
HSUM_AT = 5
TOTALS_AT = 7
EXP_AT = 1
RESIDUAL_AT, MOMENTS_AT, RESULT_AT = 3, 4, 6
YW = P + 1
HW = P + 2
YS = 132
BANK = 512
SLOT = 256

ALPHA = 0.2
LIFT = 60.0
CUT = float(np.exp(np.float64(LIFT + 1.0)))
STEEP = 1.0e6
EPS = 1e-5


def gat_layer(nc, x_rows, x_cols, packed, adj, out, r_dram):
    with ExitStack() as ctx:
        def sb(name, shape, dt=F32):
            return ctx.enter_context(nc.sbuf_tensor(name, shape, dt))

        def sem(name):
            return ctx.enter_context(nc.semaphore(name))

        xT = sb("xT", [P, N])
        weights = sb("weights", [P, 3 * P + 4])
        wT, a_sb = weights[:, 0:P], weights[:, P:P + 2]
        w_ext, ident = weights[:, P + 2:2 * P + 4], weights[:, 2 * P + 4:3 * P + 4]
        ones_row = sb("ones_row", [1, P])
        ones_sq = sb("ones_sq", [P, P])
        wa = sb("wa", [P, 2])
        wa1_wide = sb("wa1_wide", [P, P])
        x_copy = sb("x_copy", [P, ROWS])
        x_part = sb("x_part", [P, CHUNKS])
        x_pair = sb("x_pair", [P, 2])
        x_sum = sb("x_sum", [P, 1])
        warm = sb("warm", [P, BANK], BF16)
        table_junk = sb("table_junk", [P, 1])
        x_sum_wide = sb("x_sum_wide", [P, P])
        s2 = sb("s2", [P, STEPS])
        s1 = sb("s1", [P, STEPS])
        r_cols = sb("r_cols", [P, STEPS])
        r_turned_sb = sb("r_turned_sb", [STEPS, P])
        part_max = sb("part_max", [P, 1])
        top_one = sb("top_one", [1, 1])
        q_bias = sb("q_bias", [P, 1])
        f_bias = sb("f_bias", [P, 1])
        q = sb("q", [P, STEPS])
        f = sb("f", [P, STEPS])
        r = sb("r", [P, N])
        h_sum = sb("h_sum", [P, P])
        y = sb("y", [P, STEPS * YS])
        adj_ring = sb("adj_ring", [P, ADJ_RING, PAIR, ROWS], I32)
        mask_ring = sb("mask_ring", [P, MASK_RING, PAIR, ROWS], BF16)
        p_ring = sb("p_ring", [P, P_RING, ROWS])
        x_sb = sb("x_sb", [P, 2, ROWS])
        empty = sb("empty", [P, TILES])
        total = sb("total", [P, TILES])
        scale = sb("scale", [P, TILES])
        num = sb("num", [P, ROWS])
        h_new = sb("h_new", [P, ROWS])
        exp_h = sb("exp_h", [P, ROWS])
        part_sum = sb("part_sum", [P, ROWS])
        resid = sb("resid", [P, ROWS])
        stats = sb("stats", [P, TILES, 6])
        moments = sb("moments", [P, TILES, 2])
        eps_col = sb("eps_col", [P, 1])
        sigm_bias = sb("sigm_bias", [P, 1])
        var_eps = sb("var_eps", [P, TILES])
        power = sb("power", [P, TILES])
        rstd = sb("rstd", [P, TILES])
        res = sb("res", [P, 2, ROWS])

        ps = ctx.enter_context(nc.psum_tensor("ps", [P, 8 * BANK], F32))

        def acc(chunk):
            half = (chunk % 2) * 4 * BANK
            return ps[:, half:half + 4 * BANK].rearrange("p (n c) -> p n c", c=SLOT)

        y3 = y[:, :].rearrange("p (t c) -> p t c", c=YS)

        small_bank = ps[:, 3 * BANK:4 * BANK]
        wa_ps = small_bank[:, 0:2]
        top_ps = small_bank[:, 2:3]
        max_ps = small_bank[0:1, P:2 * P]
        s1_ps = ps[:, 0:ROWS]
        r_turned_ps = ps[0:STEPS, 4 * BANK:4 * BANK + P]
        hsum_ps = ps[:, 5 * BANK:5 * BANK + P]
        warm_ps = ps[:, 0:BANK]

        w_landed = sem("w_landed")
        xT_landed = [sem(f"xT_landed{c}") for c in range(CHUNKS)]
        adj_landed = [sem(f"adj_landed{s}") for s in range(ADJ_RING)]
        x_landed = [sem("x_landed0"), sem("x_landed1")]
        stored = [sem("stored0"), sem("stored1")]
        last_stored = sem("last_stored")
        consts_set = sem("consts_set")
        wa_summed = sem("wa_summed")
        wa_copied = sem("wa_copied")
        wa1_spread = sem("wa1_spread")
        xsum_done = sem("xsum_done")
        xsum_added = sem("xsum_added")
        xsum_spread = sem("xsum_spread")
        s2_copied = sem("s2_copied")
        part_max_done = sem("part_max_done")
        max_turned = sem("max_turned")
        top_found = sem("top_found")
        top_spread = sem("top_spread")
        bias_ready = sem("bias_ready")
        qf_ready = sem("qf_ready")
        s1_summed = sem("s1_summed")
        s1_copied = sem("s1_copied")
        r_cols_raw = sem("r_cols_raw")
        r_cols_cut = sem("r_cols_cut")
        r_turned = sem("r_turned")
        r_rows_ready = sem("r_rows_ready")
        r_stored = sem("r_stored")
        r_landed = sem("r_landed")
        r_raw = sem("r_raw")
        r_ready = sem("r_ready")
        hsum_summed = sem("hsum_summed")
        hsum_copied = sem("hsum_copied")
        h_summed = sem("h_summed")
        h_copied = [sem("h_copied_even"), sem("h_copied_odd")]
        y_ready = sem("y_ready")
        warm_set = sem("warm_set")
        wa_set = sem("wa_set")
        first_mask = sem("first_mask")
        mask_ready = sem("mask_ready")
        p_ready = sem("p_ready")
        half_ready = sem("half_ready")
        p_used = sem("p_used")
        last_sums = sem("last_sums")
        empty_found = sem("empty_found")
        total_done = sem("total_done")
        scale_ready = sem("scale_ready")
        num_ready = sem("num_ready")
        h_new_ready = sem("h_new_ready")
        exp_ready = sem("exp_ready")
        part_ready = sem("part_ready")
        resid_ready = sem("resid_ready")
        stats_ready = sem("stats_ready")
        moments_ready = sem("moments_ready")
        var_ready = sem("var_ready")
        rstd_ready = sem("rstd_ready")
        res_ready = sem("res_ready")
        last_res_ready = sem("last_res_ready")

        block = ctx.enter_context(nc.Block())

        @block.sync
        def _(sp):
            sp.dma_start(weights[:], packed).then_inc(w_landed, 16)
            for c in range(CHUNKS):
                sp.dma_start(xT[:, c * ROWS:(c + 1) * ROWS], x_cols[:, c * ROWS:(c + 1) * ROWS]).then_inc(xT_landed[c], 16)
            for s in range(ADJ_RING):
                sp.dma_start(adj_ring[:, s], adj[s]).then_inc(adj_landed[s], 16)
            with sp.Fori(1, CHUNKS * TURNS) as turn:
                for s in range(BODY):
                    sp.wait_ge(mask_ready, turn * BODY + (s - ADJ_RING + 1))
                    sp.dma_start(adj_ring[:, s], adj[bass.ds(turn * BODY + s, 1)].rearrange("u p k i -> p (u k) i")
                                 ).then_inc(adj_landed[s], 16)
            for g in range(GROUPS):
                cols = slice(g * GROUP * P, (g + 1) * GROUP * P)
                sp.wait_ge(last_res_ready, g + 1)
                sp.dma_start(out[CHUNKS - 1][:, cols], res[:, (CHUNKS - 1) % 2, cols]).then_inc(last_stored, 16)
            sp.wait_ge(last_stored, 16 * GROUPS)

        @block.gpsimd
        def _(pool):
            pool.wait_ge(xsum_done, CHUNKS)
            nc.gpsimd.tensor_tensor(x_pair[:], x_part[:, 0:2], x_part[:, 2:4], ALU.add).then_inc(xsum_added, 1)
            pool.wait_ge(xsum_added, 1)
            nc.gpsimd.tensor_tensor(x_sum[:], x_pair[:, 0:1], x_pair[:, 1:2], ALU.add).then_inc(xsum_added, 1)
            pool.wait_ge(xsum_added, 2)
            pool.wait_ge(consts_set, 1)
            nc.gpsimd.tensor_scalar(x_sum_wide[:], ones_sq[:], x_sum[:], None, ALU.mult).then_inc(xsum_spread, 1)

            def make_y(tiles):
                nc.gpsimd.tensor_tensor(y3[:, tiles, 0:P], y3[:, tiles, 0:P],
                                        f[:, tiles].unsqueeze(2).broadcast_to([P, tiles.stop - tiles.start, P]), ALU.mult
                                        ).then_inc(y_ready, 1)

            pool.wait_ge(qf_ready, 2)
            pool.wait_ge(h_copied[0], 1)
            make_y(slice(0, 1))
            pool.wait_ge(s2_copied, 2)
            pool.wait_ge(h_copied[0], 2)
            pool.wait_ge(h_copied[1], 2)
            nc.gpsimd.tensor_copy(y3[:, :, P], f[:]).then_inc(y_ready, 1)
            make_y(slice(1, TILES))

            pool.wait_ge(r_rows_ready, 1)
            pool.dma_start(r_dram, r_turned_sb[:]).then_inc(r_stored, 16)
            for c in range(1, CHUNKS):
                make_y(slice(c * TILES, (c + 1) * TILES))
                if c == 1:
                    pool.wait_ge(r_stored, 16)
                    r_line = r_dram.rearrange("t p -> (t p)").unsqueeze(0)
                    pool.dma_start(r[:, ROWS:N], r_line[:, ROWS:N].broadcast_to([P, N - ROWS])).then_inc(r_landed, 16)
            for c in range(2):
                pool.dma_start(x_sb[:, c], x_rows[c]).then_inc(x_landed[c], 16)

            def rows_of(tensor, tiles):
                return tensor[:, tiles[0] * P:(tiles[-1] + 1) * P]

            def new_h(g, before, tiles):
                t = slice(tiles[0], tiles[-1] + 1)
                pool.wait_ge(scale_ready, g + 1)
                pool.wait_ge(num_ready, g + 1)
                if before:
                    pool.wait_ge(resid_ready, before)
                nc.gpsimd.tensor_tensor(rows_of(h_new, tiles).rearrange("p (n c) -> p n c", c=P),
                                        rows_of(num, tiles).rearrange("p (n c) -> p n c", c=P),
                                        scale[:, t].unsqueeze(2).broadcast_to([P, len(tiles), P]), ALU.mult
                                        ).then_inc(h_new_ready, 1)

            def inverse_deviation(g, before, tiles):
                t = slice(tiles[0], tiles[-1] + 1)
                pool.wait_ge(moments_ready, g + 1)
                nc.gpsimd.tensor_scalar(var_eps[:, t], moments[:, t, 1], EPS, None, ALU.add).then_inc(var_ready, 1)
                pool.wait_ge(var_ready, g + 1)
                if before:
                    pool.wait_ge(res_ready, before)
                nc.gpsimd.tensor_tensor(rstd[:, t], var_eps[:, t], power[:, t], ALU.pow).then_inc(rstd_ready, 1)

            for c in range(CHUNKS - 1):
                new_h(c, c, range(TILES))
                pool.wait_ge(part_ready, c + 1)
                if c + 2 < CHUNKS:
                    pool.dma_start(x_sb[:, c % 2], x_rows[c + 2]).then_inc(x_landed[c % 2], 16)
                inverse_deviation(c, c, range(TILES))
                pool.wait_ge(res_ready, c + 1)
                pool.dma_start(out[c], res[:, c % 2]).then_inc(stored[c % 2], 16)
            groups = [range(g * GROUP, (g + 1) * GROUP) for g in range(GROUPS)]
            for g in range(GROUPS):
                new_h(CHUNKS - 1 + g, CHUNKS - 1, groups[g])
                inverse_deviation(CHUNKS - 1 + g, CHUNKS - 1, groups[g])
            pool.wait_ge(stored[0], 32)
            pool.wait_ge(stored[1], 16)

        @block.scalar
        def _(act):
            act.wait_ge(consts_set, 1)
            nc.scalar.activation(table_junk[:], eps_col[:], ACT.Exp)

            def sum_of_x(c):
                act.wait_ge(xT_landed[c], 16)
                if c >= 1:
                    act.wait_ge(xsum_done, c)
                nc.scalar.activation(x_copy[:], xT[:, c * ROWS:(c + 1) * ROWS], ACT.Identity, accum_out=x_part[:, c:c + 1]
                                     ).then_inc(xsum_done, 1)

            def copy_h(c):
                act.wait_ge(h_summed, c + 1)
                nc.scalar.copy(y3[:, c * TILES:(c + 1) * TILES, 0:HW], acc(c)[:, :, 0:HW]).then_inc(h_copied[1], 1)

            for c in range(3):
                sum_of_x(c)
            copy_h(1)
            sum_of_x(3)
            act.wait_ge(s2_copied, 2)
            copy_h(3)

            act.wait_ge(bias_ready, 2)
            for half in range(2):
                cols = slice(half * HALF, (half + 1) * HALF)
                act.wait_ge(s1_summed, half + 1)
                nc.scalar.activation(r[:, cols], s1_ps[:, cols], ACT.Exp, bias=q_bias[:], scale=-(1.0 - ALPHA)).then_inc(r_raw, 1)
                if half == 0:
                    act.wait_ge(s2_copied, 2)
                    nc.scalar.activation(q[:], s2[:], ACT.Exp, bias=q_bias[:], scale=1.0 - ALPHA).then_inc(qf_ready, 1)
                    nc.scalar.activation(f[:], s2[:], ACT.Exp, bias=f_bias[:], scale=ALPHA).then_inc(qf_ready, 1)
            act.wait_ge(s1_copied, 1)
            nc.scalar.activation(r_cols[:], s1[:], ACT.Exp, bias=q_bias[:], scale=-(1.0 - ALPHA)).then_inc(r_cols_raw, 1)

            def mask(s, landed, count=1):
                act.wait_ge(adj_landed[s], landed)
                nc.scalar.activation(mask_ring[:, s], adj_ring[:, s], ACT.Sigmoid,
                                     bias=sigm_bias[:], scale=STEEP).then_inc(mask_ready, count)

            def exp_of_h(g, before, tiles):
                cols = slice(tiles[0] * P, (tiles[-1] + 1) * P)
                act.wait_ge(h_new_ready, g + 1)
                if before:
                    act.wait_ge(part_ready, before)
                nc.scalar.activation(exp_h[:, cols], h_new[:, cols], ACT.Exp).then_inc(exp_ready, 1)

            for c in range(CHUNKS):
                for s in range(BODY):
                    unit = c * UNITS + s
                    if unit == 0:
                        act.wait_ge(first_mask, PAIR)
                        continue
                    if unit >= MASK_RING:
                        act.wait_ge(p_ready, PAIR * (unit - MASK_RING + 1))
                    mask(s, 16 * (c * TURNS + 1), 2 if unit == 1 else 1)

                def turn_of_masks(turn, exp_of=None):
                    for s in range(BODY):
                        act.wait_ge(p_ready, turn * (PAIR * BODY) + PAIR * (s - MASK_RING + 1))
                        mask(s, turn * 16 + 16)
                        if exp_of is not None and s == EXP_AT:
                            exp_of_h(exp_of, exp_of, range(TILES))

                if c >= 1:
                    turn_of_masks(c * TURNS + 1, c - 1)
                with act.Fori(c * TURNS + (2 if c >= 1 else 1), (c + 1) * TURNS) as turn:
                    turn_of_masks(turn)
            nc.scalar.activation(table_junk[:], eps_col[:], ACT.Exp)
            for g in range(GROUPS):
                act.wait_ge(scale_ready, CHUNKS + g)
                act.wait_ge(num_ready, CHUNKS + g)
                act.wait_ge(part_ready, CHUNKS - 1)
                for n in range(g * GROUP, (g + 1) * GROUP):
                    e = nc.scalar.activation(exp_h[:, n * P:(n + 1) * P], num[:, n * P:(n + 1) * P], ACT.Exp,
                                             scale=scale[:, n:n + 1])
                e.then_inc(exp_ready, 1)

        @block.vector
        def _(dve):
            nc.vector.memset(warm[:], 0.0).then_inc(warm_set, 1)
            nc.vector.memset(ones_row[:], 1.0)
            nc.vector.memset(power[:], -0.5)
            nc.vector.memset(ones_sq[:], 1.0)
            nc.vector.memset(sigm_bias[:], -0.5 * STEEP)
            nc.vector.memset(eps_col[:], EPS).then_inc(consts_set, 1)
            dve.wait_ge(wa_summed, 1)
            nc.vector.tensor_copy(wa[:], wa_ps).then_inc(wa_copied, 1)
            dve.wait_ge(wa_copied, 1)
            dve.wait_ge(consts_set, 1)
            nc.vector.tensor_copy(w_ext[:, P:HW], wa[:]).then_inc(wa_set, 1)
            nc.vector.tensor_scalar(wa1_wide[:], ones_sq[:], wa[:, 1:2], None, ALU.mult).then_inc(wa1_spread, 1)
            for c in (0, 2):
                dve.wait_ge(h_summed, c + 1)
                nc.vector.tensor_copy(y3[:, c * TILES:(c + 1) * TILES, 0:HW], acc(c)[:, :, 0:HW]).then_inc(h_copied[0], 1)

            def first_mask_of(k):
                dve.wait_ge(adj_landed[0], 16)
                nc.vector.tensor_scalar(mask_ring[:, 0, k], adj_ring[:, 0, k], 0.0, None, ALU.is_gt).then_inc(first_mask, 1)

            early, late = slice(0, STEPS - TILES), slice(STEPS - TILES, STEPS)
            dve.wait_ge(h_copied[0], 2)
            dve.wait_ge(h_copied[1], 1)
            nc.vector.tensor_copy(s2[:, early], y3[:, early, P]).then_inc(s2_copied, 1)
            dve.wait_ge(h_summed, CHUNKS)
            nc.vector.tensor_copy(s2[:, late], acc(CHUNKS - 1)[:, :, P]).then_inc(s2_copied, 1)
            dve.wait_ge(s2_copied, 2)
            nc.vector.reduce_max(part_max[:], s2[:], AX.X).then_inc(part_max_done, 1)
            first_mask_of(0)
            dve.wait_ge(max_turned, 1)
            nc.vector.reduce_max(top_one[:], max_ps, AX.X).then_inc(top_found, 1)
            first_mask_of(1)
            dve.wait_ge(top_spread, 1)
            nc.vector.tensor_scalar(q_bias[:], top_ps, -(1.0 - ALPHA), LIFT, ALU.mult, ALU.add).then_inc(bias_ready, 1)
            nc.vector.tensor_scalar(f_bias[:], top_ps, -ALPHA, None, ALU.mult).then_inc(bias_ready, 1)
            dve.wait_ge(h_copied[1], 2)
            nc.vector.tensor_copy(s1[:], y3[:, :, YW]).then_inc(s1_copied, 1)

            def weigh(rows, k, q_col):
                m = mask_ring[:, (k // PAIR) % MASK_RING, k % PAIR]
                nc.vector.scalar_tensor_tensor(p_ring[:, k % P_RING], rows, q_col, m, ALU.max, ALU.mult).then_inc(p_ready, 1)

            for half in range(2):
                cols = slice(half * HALF, (half + 1) * HALF)
                dve.wait_ge(r_raw, half + 1)
                nc.vector.tensor_scalar(r[:, cols], r[:, cols], CUT, None, ALU.min).then_inc(r_ready, 1)
                if half == 0:
                    dve.wait_ge(qf_ready, 1)
                    dve.wait_ge(first_mask, 1)
                dve.wait_ge(r_ready, half + 1)
                nc.vector.scalar_tensor_tensor(p_ring[:, 0, cols], r[:, cols], q[:, 0:1], mask_ring[:, 0, 0, cols],
                                               ALU.max, ALU.mult).then_inc((half_ready, p_ready)[half], 1)
            dve.wait_ge(r_cols_raw, 1)
            nc.vector.tensor_scalar(r_cols[:], r_cols[:], CUT, None, ALU.min).then_inc(r_cols_cut, 1)

            def totals(c, g, before, tiles):
                a = acc(c)
                t = slice(tiles[0], tiles[-1] + 1)
                nc.vector.tensor_scalar(empty[:, t], a[:, t, P], 0.0, None, ALU.is_equal).then_inc(empty_found, 1)
                dve.wait_ge(empty_found, g + 1)
                nc.vector.scalar_tensor_tensor(total[:, t], empty[:, t], float(N), a[:, t, P], ALU.mult, ALU.add
                                               ).then_inc(total_done, 1)
                dve.wait_ge(hsum_copied, 1)
                if before:
                    dve.wait_ge(h_new_ready, before)
                for n in tiles:
                    if n == tiles[1]:
                        dve.wait_ge(total_done, g + 1)
                        nc.vector.reciprocal(scale[:, t], total[:, t]).then_inc(scale_ready, 1)
                    u = nc.vector.scalar_tensor_tensor(num[:, n * P:(n + 1) * P], h_sum[:], empty[:, n:n + 1], a[:, n, 0:P],
                                                       ALU.mult, ALU.add)
                u.then_inc(num_ready, 1)

            def residual(g, c, tiles):
                cols = slice(tiles[0] * P, (tiles[-1] + 1) * P)
                dve.wait_ge(exp_ready, g + 1)
                dve.wait_ge(x_landed[c % 2], 16 * (c // 2 + 1))
                nc.vector.scalar_tensor_tensor(part_sum[:, cols], exp_h[:, cols], 1.0, x_sb[:, c % 2, cols], ALU.min, ALU.add
                                               ).then_inc(part_ready, 1)
                dve.wait_ge(part_ready, g + 1)
                nc.vector.scalar_tensor_tensor(resid[:, cols], h_new[:, cols], 0.0, part_sum[:, cols], ALU.max, ALU.add
                                               ).then_inc(resid_ready, 1)

            def row_moments(g, tiles):
                dve.wait_ge(resid_ready, g + 1)
                for n in tiles:
                    u = nc.vector.bn_stats(stats[:, n], resid[:, n * P:(n + 1) * P])
                u.then_inc(stats_ready, 1)
                dve.wait_ge(stats_ready, g + 1)
                for n in tiles:
                    u = nc.vector.bn_aggr(moments[:, n], stats[:, n])
                u.then_inc(moments_ready, 1)

            def normalise(c, tiles):
                for n in tiles:
                    cols = slice(n * P, (n + 1) * P)
                    u = nc.vector.tensor_scalar(res[:, c % 2, cols], resid[:, cols], moments[:, n, 0:1], rstd[:, n:n + 1],
                                                ALU.subtract, ALU.mult)
                return u

            for c in range(CHUNKS):
                rows = r[:, c * ROWS:(c + 1) * ROWS]
                if c == 1:
                    dve.wait_ge(r_landed, 16)
                for k in range(PAIR * BODY):
                    step = c * STEPS + k
                    if step == 0:
                        continue
                    if step == 1:
                        dve.wait_ge(first_mask, 2)
                    if step % PAIR == 0:
                        dve.wait_ge(mask_ready, step // PAIR + 1)
                    if step >= P_RING:
                        dve.wait_ge(p_used, step - P_RING + 1)
                    weigh(rows, k, q[:, k:k + 1])
                    if step == 1:
                        dve.wait_ge(r_turned, 1)
                        nc.vector.tensor_copy(r_turned_sb[:], r_turned_ps).then_inc(r_rows_ready, 1)
                    if c >= 1 and k == TOTALS_AT:
                        dve.wait_ge(p_used, c * STEPS)
                        totals(c - 1, c - 1, c - 1, range(TILES))

                def turn_of_steps(turn, between):
                    for k in range(PAIR * BODY):
                        if k % PAIR == 0:
                            dve.wait_ge(mask_ready, turn * BODY + (c * UNITS + k // PAIR + 1))
                        dve.wait_ge(p_used, turn * (PAIR * BODY) + (c * STEPS + k - P_RING + 1))
                        weigh(rows, k, q[:, bass.ds(turn * (PAIR * BODY) + k, 1)])
                        if between:
                            between(k)

                def last_stages(k):
                    if k == RESIDUAL_AT:
                        residual(c - 1, c - 1, range(TILES))
                    if k == MOMENTS_AT:
                        row_moments(c - 1, range(TILES))
                    if k == RESULT_AT:
                        dve.wait_ge(rstd_ready, c)
                        if c - 1 >= 2:
                            dve.wait_ge(stored[(c - 1) % 2], 16 * ((c - 1) // 2))
                        normalise(c - 1, range(TILES)).then_inc(res_ready, 1)

                if c >= 1:
                    turn_of_steps(1, last_stages)
                with dve.Fori(2 if c >= 1 else 1, TURNS) as turn:
                    turn_of_steps(turn, None)

                if c == 0:
                    dve.wait_ge(hsum_summed, 1)
                    nc.vector.tensor_copy(h_sum[:], hsum_ps).then_inc(hsum_copied, 1)

            c = CHUNKS - 1

            groups = [range(g * GROUP, (g + 1) * GROUP) for g in range(GROUPS)]
            for g in range(GROUPS + 1):
                if g < GROUPS:
                    dve.wait_ge(last_sums, g + 1)
                    totals(c, c + g, c, groups[g])
                if g >= 1:
                    dve.wait_ge(rstd_ready, c + g)
                    if g == 1:
                        dve.wait_ge(stored[c % 2], 16)
                    normalise(c, groups[g - 1]).then_inc(last_res_ready, 1)
                if g < GROUPS:
                    dve.wait_ge(h_new_ready, c + g + 1)
                    residual(c + g, c, groups[g])
                    row_moments(c + g, groups[g])

        @block.tensor
        def _(pe):
            pe.wait_ge(warm_set, 1)
            for _ in range(WARMING):
                nc.tensor.matmul(warm_ps, warm[:, 0:P], warm[:], start=True, stop=True)
            pe.wait_ge(w_landed, 16)
            nc.tensor.matmul(wa_ps, wT, a_sb, start=True, stop=True).then_inc(wa_summed, 1)
            for _ in range(2):
                nc.tensor.matmul(warm_ps, warm[:, 0:P], warm[:], start=True, stop=True)

            pe.wait_ge(wa_set, 1)
            for c in range(CHUNKS):
                pe.wait_ge(xT_landed[c], 16)
                if c >= 2:
                    pe.wait_ge(h_copied[c % 2], 1)
                for n in range(TILES):
                    t = c * TILES + n
                    m = nc.tensor.matmul(acc(c)[:, n, 0:HW], xT[:, t * P:(t + 1) * P], w_ext, start=True, stop=True)
                m.then_inc(h_summed, 1)
            pe.wait_ge(wa1_spread, 1)
            pe.wait_ge(h_copied[0], 2)
            for quarter in range(4):
                cols = slice(quarter * HALF // 2, (quarter + 1) * HALF // 2)
                m = nc.tensor.matmul(s1_ps[:, cols], wa1_wide[:], xT[:, cols], start=True, stop=True)
                if quarter % 2 == 1:
                    m.then_inc(s1_summed, 1)
                if quarter == 1:
                    pe.wait_ge(part_max_done, 1)
                    nc.tensor.transpose(max_ps, part_max[:], ident).then_inc(max_turned, 1)
                if quarter == 2:
                    pe.wait_ge(consts_set, 1)
                    pe.wait_ge(top_found, 1)
                    nc.tensor.matmul(top_ps, ones_row[:], top_one[:], start=True, stop=True).then_inc(top_spread, 1)

            def add_up(c, k, tiles, y_tile, first):
                for n in tiles:
                    m = nc.tensor.matmul(acc(c)[:, n, 0:YW], p_ring[:, k % P_RING, n * P:(n + 1) * P], y_tile,
                                         start=(first and n % 2 == 0), stop=True, skip_group_check=True)
                return m

            for c in range(CHUNKS):
                if c == 1:
                    pe.wait_ge(hsum_copied, 1)
                if c >= 2:
                    pe.wait_ge(num_ready, c - 1)
                for k in range(PAIR * BODY):
                    tiles = range(TILES)
                    if c == 0 and k == 0:
                        pe.wait_ge(y_ready, 2)
                        pe.wait_ge(bias_ready, 2)
                        pe.wait_ge(r_raw, 2)
                        pe.wait_ge(half_ready, 1)
                        add_up(c, k, range(TILES // 2), y3[:, k, 0:YW], True)
                        tiles = range(TILES // 2, TILES)
                    if c == 0 and k == 1:
                        pe.wait_ge(y_ready, 3)
                    pe.wait_ge(p_ready, c * STEPS + k + 1)
                    add_up(c, k, tiles, y3[:, k, 0:YW], k == 0).then_inc(p_used, 1)
                    if c == 0 and k == 0:
                        pe.wait_ge(r_cols_cut, 1)
                        pe.wait_ge(h_copied[1], 2)
                        nc.tensor.transpose(r_turned_ps, r_cols[:], ident).then_inc(r_turned, 1)
                    if c == 0 and k == HSUM_AT:
                        pe.wait_ge(xsum_spread, 1)
                        nc.tensor.matmul(hsum_ps, x_sum_wide[:], w_ext[:, 0:P], start=True, stop=True
                                         ).then_inc(hsum_summed, 1)
                if c == 0:
                    pe.wait_ge(y_ready, CHUNKS + 2)
                turns = TURNS - 1 if c == CHUNKS - 1 else TURNS
                with pe.Fori(1, turns) as turn:
                    for k in range(PAIR * BODY):
                        pe.wait_ge(p_ready, turn * (PAIR * BODY) + (c * STEPS + k + 1))
                        add_up(c, k, range(TILES), y[:, bass.ds(turn * (PAIR * BODY * YS) + k * YS, YW)], False
                               ).then_inc(p_used, 1)
            c = CHUNKS - 1
            for k in range(STEPS - PAIR * BODY, STEPS - GROUPED):
                pe.wait_ge(p_ready, c * STEPS + k + 1)
                add_up(c, k, range(TILES), y3[:, k, 0:YW], False).then_inc(p_used, 1)
            for g in range(GROUPS):
                for k in range(STEPS - GROUPED, STEPS):
                    if g == 0:
                        pe.wait_ge(p_ready, c * STEPS + k + 1)
                    m = add_up(c, k, range(g * GROUP, (g + 1) * GROUP), y3[:, k, 0:YW], False)
                m.then_inc(last_sums, 1)


def kernel(x, adj, L0_gnn_W, L0_gnn_a):
    import concourse.bacc as bacc
    from concourse.bass_utils import run_bass_kernel_spmd

    x, adj, W, a = (np.asarray(v) for v in (x, adj, L0_gnn_W, L0_gnn_a))
    v = adj.reshape(CHUNKS, P, TILES, CHUNKS, P, TILES // PAIR, PAIR)
    v = np.ascontiguousarray(v.transpose(0, 3, 5, 4, 6, 2, 1)).reshape(CHUNKS * UNITS, P, PAIR, ROWS)
    arrays = {
        "x_rows": x.reshape(CHUNKS, P, ROWS),
        "x_cols": np.ascontiguousarray(x.reshape(CHUNKS, P, TILES, P).transpose(3, 0, 2, 1)).reshape(P, N),
        "packed": np.concatenate([W.T, a.reshape(2, P)[::-1].T, W, np.zeros((P, 2), np.float32), np.eye(P, dtype=np.float32)], axis=1),
        "adj": v,
    }
    nc = bacc.Bacc("TRN2", target_bir_lowering=False, num_devices=1)
    aps = [nc.dram_tensor(n, list(v.shape), mybir.dt.from_np(v.dtype), kind="ExternalInput").ap() for n, v in arrays.items()]
    out = nc.dram_tensor("out", [CHUNKS, P, ROWS], F32, kind="ExternalOutput").ap()
    r_dram = nc.dram_tensor("r_dram", [STEPS, P], F32, kind="Internal").ap()
    gat_layer(nc, *aps, out, r_dram)
    result = run_bass_kernel_spmd(nc, [arrays], core_ids=[0])
    return result.results[0]["out"].reshape(N, P)
```
